# Optimizing a Trainium2 kernel written in Bass

```python
import numpy as np
import jax
import jax.numpy as jnp

def _softmax(x, axis=-1):
    return jax.nn.softmax(x, axis=axis)

def _gelu(x):
    return jax.nn.gelu(x, approximate=True)

def _silu(x):
    return jax.nn.silu(x)

def _sigmoid(x):
    return jax.nn.sigmoid(x)

def _layernorm(x, axis=-1, eps=1e-05):
    m = jnp.mean(x, axis=axis, keepdims=True)
    v = jnp.var(x, axis=axis, keepdims=True)
    return (x - m) / jnp.sqrt(v + eps)

def _scatter_add(tgt, idx, src, axis=0):
    return tgt.at[idx].add(src)

def _segment_sum(src, seg, n):
    return jax.ops.segment_sum(src, seg, n)
kernel_name = 'mk_adaln_ffn_d1_seqx_r8_d677cd'

def setup_inputs(seed: int=0):
    np.random.seed(seed)
    _w = jnp.asarray

    def _rec_inputs():
        import jax
        import jax.numpy as jnp
        _rk = jax.random.key(seed)
        x = -0.0003929 + 0.9999 * jax.random.normal(jax.random.fold_in(_rk, 1), (32, 32, 128), jnp.float32)
        _lenS = 32 - jax.random.randint(jax.random.fold_in(_rk, 7), (32,), 0, max(1, 32 // 4) + 1, jnp.int32)
        _lenS2 = 32 - jax.random.randint(jax.random.fold_in(_rk, 8), (32,), 0, max(1, 32 // 4) + 1, jnp.int32)
        itok_B_0_63 = jax.random.randint(jax.random.fold_in(_rk, 11), (32,), 0, 64, jnp.int32)
        return (x, itok_B_0_63)
    x, itok_B_0_63 = _rec_inputs()

    def _L0_cond_setup():
        import jax, jax.numpy as jnp
        import numpy as np
        NUM_CATEGORIES = 64
        INPUT_DIM = 128
        HIDDEN_DIM = 128
        B = 32
        S = 64
        key = jax.random.key(seed)
        kx, kc, kw = jax.random.split(key, 3)
        x = jax.random.normal(kx, (B, S, INPUT_DIM), dtype=jnp.float32)
        cat_ids = jax.random.randint(kc, (B,), 0, NUM_CATEGORIES, dtype=jnp.int32)
        W = 0.02 * jax.random.normal(kw, (NUM_CATEGORIES, INPUT_DIM, HIDDEN_DIM), dtype=jnp.float32)
        b = jnp.zeros((NUM_CATEGORIES, HIDDEN_DIM), dtype=jnp.float32)
        return {'x': x, 'cat_ids': cat_ids, 'W': W, 'b': b}
    _L0_cond_all = _L0_cond_setup()
    _L0_cond_in = {k: v for k, v in _L0_cond_all.items() if k in ('W', 'b')}
    del _L0_cond_all

    def _L0_ffn_setup():
        import jax, jax.numpy as jnp
        import numpy as np
        SWIGLU_ALPHA = 1.702
        SWIGLU_LIMIT = 7.0
        TOP_K = 4
        key = jax.random.key(seed)
        k = jax.random.split(key, 5)
        B, S, D, E, I = (2, 128, 128, 8, 256)
        return {'hidden_states': jax.random.normal(k[0], (B, S, D), dtype=jnp.float32), 'router_weight': jax.random.normal(k[1], (E, D), dtype=jnp.float32) * 0.02, 'router_bias': jnp.zeros((E,), dtype=jnp.float32), 'gate_up_proj': jax.random.normal(k[2], (E, 2 * I, D), dtype=jnp.float32) * 0.02, 'gate_up_proj_bias': jnp.zeros((E, 2 * I), dtype=jnp.float32), 'down_proj': jax.random.normal(k[3], (E, D, I), dtype=jnp.float32) * 0.02, 'down_proj_bias': jnp.zeros((E, D), dtype=jnp.float32)}
    _L0_ffn_all = _L0_ffn_setup()
    _L0_ffn_in = {k: v for k, v in _L0_ffn_all.items() if k in ('router_weight', 'router_bias', 'gate_up_proj', 'gate_up_proj_bias', 'down_proj', 'down_proj_bias')}
    del _L0_ffn_all
    return {'x': x, 'itok_B_0_63': itok_B_0_63, 'L0_cond_W': _L0_cond_in['W'], 'L0_cond_b': _L0_cond_in['b'], 'L0_ffn_router_weight': _L0_ffn_in['router_weight'], 'L0_ffn_router_bias': _L0_ffn_in['router_bias'], 'L0_ffn_gate_up_proj': _L0_ffn_in['gate_up_proj'], 'L0_ffn_gate_up_proj_bias': _L0_ffn_in['gate_up_proj_bias'], 'L0_ffn_down_proj': _L0_ffn_in['down_proj'], 'L0_ffn_down_proj_bias': _L0_ffn_in['down_proj_bias']}

def reference(x, itok_B_0_63, L0_cond_W, L0_cond_b, L0_ffn_router_weight, L0_ffn_router_bias, L0_ffn_gate_up_proj, L0_ffn_gate_up_proj_bias, L0_ffn_down_proj, L0_ffn_down_proj_bias):
    import jax
    import jax.numpy as jnp

    def _L0_cond_ref(x, cat_ids, W, b):
        import jax, jax.numpy as jnp
        import numpy as np
        NUM_CATEGORIES = 64
        INPUT_DIM = 128
        HIDDEN_DIM = 128
        B = 32
        S = 64
        selected_W = W[cat_ids]
        selected_b = b[cat_ids]
        out = jnp.einsum('bsd,bdh->bsh', x, selected_W) + selected_b[:, None, :]
        return out

    def _L0_ffn_ref(hidden_states, router_weight, router_bias, gate_up_proj, gate_up_proj_bias, down_proj, down_proj_bias):
        import jax, jax.numpy as jnp
        import numpy as np
        SWIGLU_ALPHA = 1.702
        SWIGLU_LIMIT = 7.0
        TOP_K = 4
        B, S, D = hidden_states.shape
        E = router_weight.shape[0]
        x = hidden_states.reshape(-1, D)
        N = x.shape[0]
        logits = x @ router_weight.T + router_bias
        topk_logits, topk_idx = jax.lax.top_k(logits, TOP_K)
        topk_w = jax.nn.softmax(topk_logits.astype(jnp.float32), axis=-1)
        combine = jnp.zeros((N, E), dtype=jnp.float32)
        combine = combine.at[jnp.arange(N)[:, None], topk_idx].set(topk_w)
        gate_up = jnp.einsum('nd,ejd->nej', x, gate_up_proj) + gate_up_proj_bias
        gate, up = jnp.split(gate_up, 2, axis=-1)
        gate = jnp.minimum(gate, SWIGLU_LIMIT)
        up = jnp.clip(up, -SWIGLU_LIMIT, SWIGLU_LIMIT)
        act = (up + 1.0) * gate * jax.nn.sigmoid(SWIGLU_ALPHA * gate)
        out = jnp.einsum('nei,edi->ned', act, down_proj) + down_proj_bias
        y = jnp.einsum('ned,ne->nd', out, combine.astype(out.dtype))
        return y.reshape(B, S, D)
    x = x + _L0_ffn_ref(_L0_cond_ref(x, itok_B_0_63, L0_cond_W, L0_cond_b), L0_ffn_router_weight, L0_ffn_router_bias, L0_ffn_gate_up_proj, L0_ffn_gate_up_proj_bias, L0_ffn_down_proj, L0_ffn_down_proj_bias)
    return x

_drawn_inputs = setup_inputs


def setup_inputs(seed=0):
    import zlib

    import numpy as np

    out = dict(_drawn_inputs(seed))
    spreads = {'L0_cond_b': (0.0, 0.362),
     'L0_ffn_router_bias': (0.0, 0.1),
     'L0_ffn_gate_up_proj_bias': (0.0, 0.8),
     'L0_ffn_down_proj_bias': (0.0, 0.1)}
    factors = {'L0_ffn_gate_up_proj': 8.0, 'L0_ffn_down_proj': 6.111}
    for name, (base, spread) in spreads.items():
        noise = np.random.default_rng([zlib.crc32(name.encode()), seed]).standard_normal(out[name].shape)
        drawn = base * np.exp(spread * noise) if base else spread * noise
        out[name] = jnp.asarray(drawn.astype(out[name].dtype))
    for name, factor in factors.items():
        out[name] = (out[name] * factor).astype(out[name].dtype)
    return out
```

```python
import concourse.bass as bass
from concourse import mybir
from contextlib import ExitStack

F32 = mybir.dt.float32
F32R = mybir.dt.float32r
I32 = mybir.dt.int32
ALU = mybir.AluOpType
ACT = mybir.ActivationFunctionType
AX_X = mybir.AxisListType.X

P = 128
ALPHA = 1.702
LIMIT = 7.0
TOP_K = 4


def adaln_moe_ffn_kernel(
    nc: bass.Bass,
    x_t: bass.AP,
    cat_ids: bass.AP,
    cond_w: bass.AP,
    cond_b: bass.AP,
    params: bass.AP,
    router_b: bass.AP,
    gate_up_w: bass.AP,
    down_w: bass.AP,
    consts: bass.AP,
    out_t: bass.AP,
):
    D, N = x_t.shape
    C = cond_w.shape[0]
    B = cat_ids.shape[1]
    S = N // B
    E = gate_up_w.shape[0]
    I2 = gate_up_w.shape[2]
    KT = I2 // 2 // P
    J = 2 * KT
    HALF = 512
    NH = N // HALF
    BH = HALF // S
    T = N // P
    TH = T // NH
    Q = NH * KT
    LOADS = 4
    assert D == P and N % HALF == 0 and E % 2 == 0 and BH % (2 * LOADS) == 0

    def of(e, times, plus=0):
        if isinstance(e, int):
            return times * e + plus
        k, c = e
        return k * (2 * times) + (times * c + plus)

    def after(e, more):
        return e + more if isinstance(e, int) else (e[0], e[1] + more)

    cat_scratch = nc.dram_tensor("combine_scratch", [E, N], F32, kind="Internal").ap()

    with ExitStack() as ctx:
        def sb(name, shape, dt=F32):
            return ctx.enter_context(nc.sbuf_tensor(name, shape, dt))

        def pb(name, shape):
            return ctx.enter_context(nc.psum_tensor(name, shape, F32))

        def sem(name):
            return ctx.enter_context(nc.semaphore(name))

        y = sb("y", [P, N])
        w_sel = sb("w_sel", [P, B, D])
        cb = sb("cb", [C, D])
        cat_bc = sb("cat_bc", [C, B], I32)
        cat_f = sb("cat_f", [C, B])
        onehot = sb("onehot", [C, B])
        b_sel = sb("b_sel", [P, B])
        prm = sb("prm", [P, E + E * J + E])
        rb = sb("rb", [P, E])
        cst = sb("cst", [P, P + E * E + 1])
        act_bias = sb("act_bias", [P, E, J])
        bias_now = sb("bias_now", [P, 2, J])
        h = sb("h", [P, N])
        h_hi = sb("h_hi", [P, N], F32R)
        h_lo = sb("h_lo", [P, N], F32R)
        gu_raw = sb("gu_raw", [P, 2, I2])
        gu_hi = [sb(f"gu_hi{i}", [P, I2], F32R) for i in range(2)]
        gu_lo = [sb(f"gu_lo{i}", [P, I2], F32R) for i in range(2)]
        dn = [sb(f"dn{i}", [P, KT * D]) for i in range(2)]
        gate = sb("gate", [P, 2, HALF])
        up = sb("up", [P, 2, HALF])
        z = sb("z", [P, 2, Q, HALF])
        scaled = sb("scaled", [P, NH, HALF])
        lg = sb("lg", [P, T, E])
        gt = sb("gt", [P, T, E, E])
        eq = sb("eq", [P, T, E, E])
        rank = sb("rank", [P, T, E])
        chosen = sb("chosen", [P, T, E])
        top = sb("top", [P, T])
        shifted = sb("shifted", [P, T, E])
        expd = sb("expd", [P, T, E])
        kept = sb("kept", [P, T, E])
        denom = sb("denom", [P, T])
        rdenom = sb("rdenom", [P, T])
        comb = sb("comb", [P, T, E])
        comb_t = sb("comb_t", [E, N])
        comb_bc = sb("comb_bc", [P, E, N])

        gate_ps = pb("gate_ps", [P, 2, HALF])
        up_ps = pb("up_ps", [P, 2, HALF])
        down_ps = pb("down_ps", [P, NH, HALF])
        misc_ps = pb("misc_ps", [P, 2, HALF])
        lg_ps = misc_ps[:, 0, 0:T * E].rearrange("p (t e) -> p t e", e=E)
        bsel_ps = misc_ps[:, 1, 0:B]

        router_w = prm[:, 0:E]
        gub = prm[:, E:E + E * J].rearrange("p (e j) -> p e j", j=J)
        dnb = prm[:, E + E * J:E + E * J + E]
        ident = cst[:, 0:P]
        earlier = cst[:, P:P + E * E].rearrange("p (e j) -> p e j", e=E)
        row_no = cst[0:C, P + E * E:P + E * E + 1]

        x_loaded = [sem(f"x_loaded{i}") for i in range(NH)]
        w_loaded = [sem(f"w_loaded{i}") for i in range(NH)]
        prm_loaded = sem("prm_loaded")
        rb_loaded = sem("rb_loaded")
        cb_loaded = sem("cb_loaded")
        cat_loaded = sem("cat_loaded")
        cst_loaded = sem("cst_loaded")
        gu_loaded = [sem(f"gu_loaded{i}") for i in range(2)]
        dn_loaded = [sem(f"dn_loaded{i}") for i in range(2)]
        comb_stored = sem("comb_stored")
        comb_loaded = [sem(f"comb_loaded{i}") for i in range(2)]
        out_stored = sem("out_stored")
        cat_cast = sem("cat_cast")
        onehot_ready = sem("onehot_ready")
        bsel_ready = sem("bsel_ready")
        bsel_copied = sem("bsel_copied")
        biases_ready = sem("biases_ready")
        hps_ready = sem("hps_ready")
        hi_ready = sem("hi_ready")
        lo_ready = sem("lo_ready")
        logits_ready = sem("logits_ready")
        shifted_ready = sem("shifted_ready")
        exp_ready = sem("exp_ready")
        comb_ready = sem("comb_ready")
        combt_ready = sem("combt_ready")
        combt_copied = sem("combt_copied")
        bias_placed = sem("bias_placed")
        w_hi_ready = sem("w_hi_ready")
        w_lo_ready = sem("w_lo_ready")
        gate_ready = sem("gate_ready")
        up_ready = sem("up_ready")
        gate_done = sem("gate_done")
        up_done = sem("up_done")
        up_clamped = sem("up_clamped")
        z_done = sem("z_done")
        down_step = sem("down_step")
        down_read = sem("down_read")
        y_added = sem("y_added")
        dve_step = sem("dve_step")

        block = ctx.enter_context(nc.Block())

        @block.sync
        def _(sp):
            ids = [sp.alloc_register(f"id{i}") for i in range(LOADS)]

            def gather(half, first):
                with sp.Fori(0, BH // (2 * LOADS)) as g:
                    b = half * BH + first + g * (2 * LOADS)
                    sp.load(ids, cat_ids[0:1, bass.ds(b, LOADS)])
                    for i in range(LOADS):
                        c = sp.snap(ids[i], min_val=0, max_val=C - 1)
                        sp.dma_start(w_sel[:, bass.ds(b + i, 1), :],
                                     cond_w[bass.ds(c, 1), :, :].rearrange("c d k -> d c k")
                                     ).then_inc(w_loaded[half], 16)

            def load_gate_up(e, slot):
                sp.dma_start(gu_raw[:, slot, :],
                             gate_up_w[bass.ds(of(e, 1), 1), :, :].rearrange("e d j -> d (e j)")
                             ).then_inc(gu_loaded[slot], 16)

            def load_down(e, slot):
                sp.dma_start(dn[slot][:, :], down_w[bass.ds(of(e, 1), 1), :, :].rearrange("e p n -> p (e n)")
                             ).then_inc(dn_loaded[slot], 16)

            gather(0, 0)
            load_gate_up(0, 0)
            gather(1, 0)
            load_gate_up(1, 1)
            load_down(0, 0)
            load_down(1, 1)

            sp.wait_ge(combt_copied, 1)
            sp.dma_start(cat_scratch, comb_t[:, :]).then_inc(comb_stored, 16)
            sp.wait_ge(comb_stored, 16)
            for part, (e0, e1) in enumerate(((0, 2), (2, E))):
                sp.dma_start(comb_bc[:, e0:e1, :], cat_scratch[e0:e1, :].partition_broadcast(P)
                             ).then_inc(comb_loaded[part], 16)

            with sp.Fori(0, E // 2 - 1) as k:
                for slot in range(2):
                    e = (k, 2 + slot)
                    sp.wait_ge(w_lo_ready, of(e, 1, -1))
                    load_gate_up(e, slot)
                    sp.wait_ge(down_step, of(e, Q, -Q))
                    load_down(e, slot)

            for half in range(NH):
                sp.wait_ge(y_added, NH * (E - 1) + half + 1)
                sp.dma_start(out_t[:, half * HALF:(half + 1) * HALF],
                             y[:, half * HALF:(half + 1) * HALF]).then_inc(out_stored, 16)
            sp.wait_ge(out_stored, 16 * NH)

        def split_hi(act, e, slot):
            act.wait_ge(gu_loaded[slot], of(e, 8, 16 - 8 * slot))
            nc.scalar.copy(gu_hi[slot][:, :], gu_raw[:, slot, :]).then_inc(w_hi_ready, 1)
            nc.scalar.copy(bias_now[:, slot, :], act_bias[:, bass.ds(of(e, 1), 1), :].rearrange("p e j -> p (e j)")
                           ).then_inc(bias_placed, 1)

        @block.scalar
        def _(act):
            ids = [act.alloc_register(f"ida{i}") for i in range(LOADS)]

            def gather(half, first):
                with act.Fori(0, BH // (2 * LOADS)) as g:
                    b = half * BH + first + g * (2 * LOADS)
                    act.load(ids, cat_ids[0:1, bass.ds(b, LOADS)])
                    for i in range(LOADS):
                        c = act.snap(ids[i], min_val=0, max_val=C - 1)
                        act.dma_start(w_sel[:, bass.ds(b + i, 1), :],
                                      cond_w[bass.ds(c, 1), :, :].rearrange("c d k -> d c k")
                                      ).then_inc(w_loaded[half], 16)

            act.dma_start(y[:, 0:HALF], x_t[:, 0:HALF]).then_inc(x_loaded[0], 16)
            act.dma_start(cat_bc[:, :], cat_ids.partition_broadcast(C)).then_inc(cat_loaded, 16)
            gather(0, LOADS)
            act.dma_start(cb[:, :], cond_b).then_inc(cb_loaded, 16)
            act.dma_start(cst[:, :], consts).then_inc(cst_loaded, 16)
            act.dma_start(prm[:, :], params).then_inc(prm_loaded, 16)
            for half in range(1, NH):
                act.dma_start(y[:, half * HALF:(half + 1) * HALF],
                              x_t[:, half * HALF:(half + 1) * HALF]).then_inc(x_loaded[half], 16)
            gather(1, LOADS)
            act.dma_start(rb[:, :], router_b.partition_broadcast(P)).then_inc(rb_loaded, 16)

            def h_split(half):
                sl = slice(half * HALF, (half + 1) * HALF)
                act.wait_ge(down_read, half + 1)
                nc.scalar.copy(h_hi[:, sl], h[:, sl]).then_inc(hi_ready, 1)

            def pair(e, slot, q):
                if q == 0:
                    act.wait_ge(bias_placed, of(e, 1, 1))
                act.wait_ge(gate_ready, of(e, Q, q + 1))
                if e != 0 or q >= 2:
                    act.wait_ge(z_done, of(e, Q, q - 1))
                nc.scalar.activation(gate[:, q % 2, :], gate_ps[:, q % 2, :], ACT.Silu,
                                     bias=bias_now[:, slot, q % KT:q % KT + 1], scale=ALPHA).then_inc(gate_done, 1)
                act.wait_ge(up_ready, of(e, Q, q + 1))
                nc.scalar.activation(up[:, q % 2, :], up_ps[:, q % 2, :], ACT.Identity,
                                     bias=bias_now[:, slot, KT + q % KT:KT + q % KT + 1], scale=1.0 / ALPHA).then_inc(up_done, 1)

            act.wait_ge(biases_ready, 2)
            split_hi(act, 0, 0)
            h_split(0)
            pair(0, 0, 0)
            h_split(1)
            pair(0, 0, 1)
            act.wait_ge(shifted_ready, 1)
            nc.scalar.activation(expd[:, :, :], shifted[:, :, :], ACT.Exp).then_inc(exp_ready, 1)
            pair(0, 0, 2)
            split_hi(act, 1, 1)
            pair(0, 0, 3)

            def step(e, slot):
                for q in range(Q):
                    pair(e, slot, q)
                    if q == 1:
                        split_hi(act, after(e, 1), 1 - slot)

            with act.Fori(0, E // 2 - 1) as k:
                step((k, 1), 1)
                step((k, 2), 0)
            for q in range(Q):
                pair(E - 1, 1, q)

        @block.vector
        def _(dve):
            steps = [0]

            def link(ins):
                steps[0] += 1
                ins.then_inc(dve_step, 1)
                dve.wait_ge(dve_step, steps[0])

            def bc(ap):
                return ap.unsqueeze(2).to_broadcast([P, T, E])

            dve.wait_ge(cat_loaded, 16)
            link(nc.vector.tensor_copy(cat_f[:, :], cat_bc[:, :]))
            dve.wait_ge(cst_loaded, 16)
            nc.vector.tensor_scalar(onehot[:, :], cat_f[:, :], row_no, None, ALU.is_equal).then_inc(onehot_ready, 1)
            dve.wait_ge(prm_loaded, 16)
            nc.vector.tensor_scalar(act_bias[:, :, 0:KT], gub[:, :, 0:KT], ALPHA, None, ALU.mult).then_inc(biases_ready, 1)
            nc.vector.tensor_scalar(act_bias[:, :, KT:J], gub[:, :, KT:J], 1.0, 1.0 / ALPHA, ALU.add, ALU.mult).then_inc(biases_ready, 1)
            dve.wait_ge(bsel_ready, 1)
            nc.vector.tensor_copy(b_sel[:, :], bsel_ps).then_inc(bsel_copied, 1)

            def split_lo(e, slot):
                dve.wait_ge(w_hi_ready, of(e, 1, 1))
                nc.vector.tensor_tensor(gu_lo[slot][:, :], gu_raw[:, slot, :], gu_hi[slot][:, :].bitcast(F32),
                                        ALU.subtract).then_inc(w_lo_ready, 1)

            def h_add(half):
                sl = slice(half * HALF, (half + 1) * HALF)
                dve.wait_ge(hps_ready, half + 1)
                dve.wait_ge(bsel_copied, 1)
                nc.vector.tensor_tensor(
                    h[:, sl].rearrange("p (b s) -> p b s", s=S),
                    down_ps[:, half, :].rearrange("p (b s) -> p b s", s=S),
                    b_sel[:, half * BH:(half + 1) * BH].unsqueeze(2).to_broadcast([P, BH, S]),
                    ALU.add).then_inc(down_read, 1)

            def h_rest(half):
                sl = slice(half * HALF, (half + 1) * HALF)
                dve.wait_ge(hi_ready, half + 1)
                nc.vector.tensor_tensor(h_lo[:, sl], h[:, sl], h_hi[:, sl].bitcast(F32),
                                        ALU.subtract).then_inc(lo_ready, 1)

            def pair(e, slot, q):
                dve.wait_ge(up_done, of(e, Q, q + 1))
                nc.vector.tensor_scalar(up[:, q % 2, :], up[:, q % 2, :], (1.0 - LIMIT) / ALPHA,
                                        (1.0 + LIMIT) / ALPHA, ALU.max, ALU.min).then_inc(up_clamped, 1)
                dve.wait_ge(up_clamped, of(e, Q, q + 1))
                dve.wait_ge(gate_done, of(e, Q, q + 1))
                nc.vector.scalar_tensor_tensor(z[:, slot, q, :], gate[:, q % 2, :], SILU_AT_LIMIT,
                                               up[:, q % 2, :], ALU.min, ALU.mult).then_inc(z_done, 1)

            def add_expert(e, half):
                sl = slice(half * HALF, (half + 1) * HALF)
                dve.wait_ge(down_step, of(e, Q, KT * (half + 1)))
                nc.vector.scalar_tensor_tensor(
                    scaled[:, half, :], down_ps[:, half, :], dnb[:, bass.ds(of(e, 1), 1)],
                    comb_bc[:, bass.ds(of(e, 1), 1), sl].rearrange("p e n -> p (e n)"),
                    ALU.add, ALU.mult).then_inc(down_read, 1)
                dve.wait_ge(down_read, of(e, NH, NH + half + 1))
                nc.vector.tensor_tensor(y[:, sl], y[:, sl], scaled[:, half, :], ALU.add).then_inc(y_added, 1)

            h_add(0)
            split_lo(0, 0)
            h_rest(0)
            h_add(1)
            pair(0, 0, 0)
            h_rest(1)

            dve.wait_ge(logits_ready, 1)
            dve.wait_ge(rb_loaded, 16)
            link(nc.vector.tensor_tensor(lg[:, :, :], lg_ps, rb[:, :].unsqueeze(1).to_broadcast([P, T, E]), ALU.add))
            link(nc.vector.tensor_reduce(top[:, :], lg[:, :, :], AX_X, ALU.max))
            nc.vector.tensor_tensor(shifted[:, :, :], lg[:, :, :], bc(top[:, :]), ALU.subtract).then_inc(shifted_ready, 1)
            pair(0, 0, 1)
            other = lg[:, :, :].unsqueeze(2).to_broadcast([P, T, E, E])
            own = lg[:, :, :].unsqueeze(3).to_broadcast([P, T, E, E])
            nc.vector.tensor_tensor(gt[:, :, :, :], other, own, ALU.is_gt)
            link(nc.vector.tensor_tensor(eq[:, :, :, :], other, own, ALU.is_equal))
            link(nc.vector.tensor_tensor(eq[:, :, :, :], eq[:, :, :, :],
                                         earlier.unsqueeze(1).to_broadcast([P, T, E, E]), ALU.mult))
            link(nc.vector.tensor_tensor(gt[:, :, :, :], gt[:, :, :, :], eq[:, :, :, :], ALU.add))
            link(nc.vector.tensor_reduce(rank[:, :, :], gt[:, :, :, :], AX_X, ALU.add))
            link(nc.vector.tensor_scalar(chosen[:, :, :], rank[:, :, :], float(TOP_K), None, ALU.is_lt))
            dve.wait_ge(exp_ready, 1)
            link(nc.vector.tensor_tensor(kept[:, :, :], expd[:, :, :], chosen[:, :, :], ALU.mult))
            link(nc.vector.tensor_reduce(denom[:, :], kept[:, :, :], AX_X, ALU.add))
            link(nc.vector.reciprocal(rdenom[:, :], denom[:, :]))
            nc.vector.tensor_tensor(comb[:, :, :], kept[:, :, :], bc(rdenom[:, :]), ALU.mult).then_inc(comb_ready, 1)
            pair(0, 0, 2)
            split_lo(1, 1)
            dve.wait_ge(combt_ready, 1)
            nc.vector.tensor_copy(comb_t[:, :].rearrange("e (k n) -> e k n", k=2), misc_ps[0:E, :, :]
                                  ).then_inc(combt_copied, 1)
            pair(0, 0, 3)

            def step(e, slot, last=False):
                for q in range(Q):
                    pair(e, slot, q)
                    if q == 1 and not last:
                        split_lo(after(e, 1), 1 - slot)
                    if q % KT == KT - 1:
                        add_expert(after(e, -1), q // KT)

            dve.wait_ge(comb_loaded[0], 16)
            step(1, 1)
            dve.wait_ge(comb_loaded[1], 16)
            step(2, 0)
            with dve.Fori(0, E // 2 - 2) as k:
                step((k, 3), 1)
                step((k, 4), 0)
            step(E - 1, 1, last=True)
            for half in range(NH):
                add_expert(E - 1, half)

        @block.tensor
        def _(pe):
            pe.wait_ge(cb_loaded, 16)
            pe.wait_ge(onehot_ready, 1)
            nc.tensor.matmul(bsel_ps, cb[:, :], onehot[:, :], start=True, stop=True).then_inc(bsel_ready, 1)

            def condition(half):
                pe.wait_ge(x_loaded[half], 16)
                pe.wait_ge(w_loaded[half], 16 * BH)
                for i in range(BH):
                    b = half * BH + i
                    last = nc.tensor.matmul(down_ps[:, half, i * S:(i + 1) * S], w_sel[:, b, :],
                                            y[:, b * S:(b + 1) * S], start=True, stop=True)
                last.then_inc(hps_ready, 1)

            def logits(half):
                pe.wait_ge(down_read, half + 1)
                for t in range(half * TH, (half + 1) * TH):
                    last = nc.tensor.matmul(lg_ps[:, t, :], h[:, t * P:(t + 1) * P], router_w, start=True, stop=True)
                if half == NH - 1:
                    last.then_inc(logits_ready, 1)

            def product(ps, slot, tile, half):
                js = slice(tile * P, (tile + 1) * P)
                ns = slice(half * HALF, (half + 1) * HALF)
                nc.tensor.matmul(ps, gu_lo[slot][:, js], h_hi[:, ns], start=True, stop=False)
                nc.tensor.matmul(ps, gu_hi[slot][:, js], h_lo[:, ns], start=False, stop=False)
                return nc.tensor.matmul(ps, gu_hi[slot][:, js], h_hi[:, ns], start=False, stop=True)

            def gate_up(e, slot, q):
                half, tile = q // KT, q % KT
                first = e == 0 and q < 2
                if not first:
                    pe.wait_ge(gate_done, of(e, Q, q - 1))
                product(gate_ps[:, q % 2, :], slot, tile, half).then_inc(gate_ready, 1)
                if not first:
                    pe.wait_ge(up_done, of(e, Q, q - 1))
                product(up_ps[:, q % 2, :], slot, KT + tile, half).then_inc(up_ready, 1)

            def down(e, slot, q):
                half, tile = q // KT, q % KT
                if tile == 0:
                    pe.wait_ge(down_read, of(e, NH, half + 1))
                pe.wait_ge(z_done, of(e, Q, q + 1))
                nc.tensor.matmul(down_ps[:, half, :], dn[slot][:, tile * D:(tile + 1) * D], z[:, slot, q, :],
                                 start=(tile == 0), stop=(tile == KT - 1)).then_inc(down_step, 1)

            def weights_ready(e):
                pe.wait_ge(w_lo_ready, of(e, 1, 1))

            condition(0)
            weights_ready(0)
            pe.wait_ge(lo_ready, 1)
            gate_up(0, 0, 0)
            condition(1)
            pe.wait_ge(prm_loaded, 16)
            logits(0)
            gate_up(0, 0, 1)
            logits(1)
            pe.wait_ge(lo_ready, 2)
            gate_up(0, 0, 2)
            pe.wait_ge(comb_ready, 1)
            for t in range(T):
                last = nc.tensor.transpose(misc_ps[0:E, t // TH, (t % TH) * P:(t % TH + 1) * P], comb[:, t, :], ident)
            last.then_inc(combt_ready, 1)
            gate_up(0, 0, 3)

            def step(e, slot):
                weights_ready(e)
                pe.wait_ge(dn_loaded[1 - slot], of(after(e, -1), 8, 16 - 8 * (1 - slot)))
                for q in range(Q):
                    gate_up(e, slot, q)
                    down(after(e, -1), 1 - slot, q)

            with pe.Fori(0, E // 2 - 1) as k:
                step((k, 1), 1)
                step((k, 2), 0)
            step(E - 1, 1)
            pe.wait_ge(dn_loaded[1], 8 * (E - 2) + 16)
            for q in range(Q):
                down(E - 1, 1, q)


def _silu_at_limit():
    import math
    a = ALPHA * LIMIT
    return a / (1.0 + math.exp(-a))


SILU_AT_LIMIT = _silu_at_limit()


def kernel(x, itok_B_0_63, L0_cond_W, L0_cond_b, L0_ffn_router_weight, L0_ffn_router_bias,
           L0_ffn_gate_up_proj, L0_ffn_gate_up_proj_bias, L0_ffn_down_proj, L0_ffn_down_proj_bias):
    import numpy as np
    import concourse.bacc as bacc
    from concourse import mybir as mb
    from concourse.bass_utils import run_bass_kernel_spmd

    x = np.asarray(x)
    bsz, s, d = x.shape
    n = bsz * s
    gu = np.asarray(L0_ffn_gate_up_proj)
    dnw = np.asarray(L0_ffn_down_proj)
    e, i2, _ = gu.shape
    kt = i2 // 2 // P
    gub = np.asarray(L0_ffn_gate_up_proj_bias).reshape(e, 2 * kt, P).transpose(2, 0, 1).reshape(P, e * 2 * kt)
    shapes_only = np.concatenate([
        np.eye(P, dtype=np.float32),
        np.broadcast_to(np.tril(np.ones((e, e), np.float32), -1).reshape(1, e * e), (P, e * e)),
        np.arange(P, dtype=np.float32).reshape(P, 1)], axis=1)
    arrays = {
        "x_t": x.reshape(n, d).T,
        "cat_ids": np.asarray(itok_B_0_63).reshape(1, bsz),
        "cond_w": np.asarray(L0_cond_W),
        "cond_b": np.asarray(L0_cond_b),
        "params": np.concatenate([np.asarray(L0_ffn_router_weight).T, gub, np.asarray(L0_ffn_down_proj_bias).T], axis=1),
        "router_b": np.asarray(L0_ffn_router_bias).reshape(1, e),
        "gate_up_w": gu.transpose(0, 2, 1),
        "down_w": dnw.reshape(e, d, kt, P).transpose(0, 3, 2, 1).reshape(e, P, kt * d),
        "consts": shapes_only,
    }
    arrays = {k: np.ascontiguousarray(v) for k, v in arrays.items()}
    nc = bacc.Bacc("TRN2", target_bir_lowering=False, num_devices=1)
    args = [nc.dram_tensor(k, a.shape, mb.dt.from_np(a.dtype), kind="ExternalInput").ap() for k, a in arrays.items()]
    args.append(nc.dram_tensor("out_t", (d, n), mb.dt.float32, kind="ExternalOutput").ap())
    adaln_moe_ffn_kernel(nc, *args)
    got = run_bass_kernel_spmd(nc, [arrays], core_ids=[0]).results[0]["out_t"]
    return np.ascontiguousarray(np.asarray(got).T).reshape(bsz, s, d)
```

```python
import concourse.bass as bass
from concourse import mybir
from contextlib import ExitStack

F32 = mybir.dt.float32
F32R = mybir.dt.float32r
BF16 = mybir.dt.bfloat16
I32 = mybir.dt.int32
ALU = mybir.AluOpType
ACT = mybir.ActivationFunctionType
AX_X = mybir.AxisListType.X

P = 128
ALPHA = 1.702
LIMIT = 7.0
TOP_K = 4
WARM_UP = 10
FILL = [[0, 5, 3, 2], [1, 1, 1, 1]]
WHILE_SPLIT = 5


def adaln_moe_ffn_kernel(
    nc: bass.Bass,
    x_t: bass.AP,
    cat_ids: bass.AP,
    cond_w: bass.AP,
    params: bass.AP,
    gate_up_w: bass.AP,
    down_w: bass.AP,
    out_t: bass.AP,
):
    D, N = x_t.shape
    C = cond_w.shape[0]
    B = cat_ids.shape[1]
    S = N // B
    E = gate_up_w.shape[0]
    I2 = gate_up_w.shape[2]
    KT = I2 // 2 // P
    J = 2 * KT
    HALF = 512
    NH = N // HALF
    BH = HALF // S
    T = N // P
    TH = T // NH
    Q = NH * KT
    GH = BH // 4
    GROUPS = NH * GH
    SHARE = [{"sp": [2, 1, 1, 1], "act": [1, 2, 1, 1], "pool": [1, 1, 2, 2]},
             {"sp": [2, 2, 2, 2], "act": [0, 0, 0, 0], "pool": [2, 2, 2, 2]}]
    QUEUES = ("sp", "act", "pool")
    assert D == P and N == NH * HALF and NH == 2 and KT == 2 and E % 2 == 0 and E >= 6 and BH % 4 == 0

    def of(e, times, plus=0):
        if isinstance(e, int):
            return times * e + plus
        k, c = e
        return k * (2 * times) + (times * c + plus)

    def after(e, more):
        return e + more if isinstance(e, int) else (e[0], e[1] + more)

    with ExitStack() as ctx:
        def sb(name, shape, dt=F32):
            return ctx.enter_context(nc.sbuf_tensor(name, shape, dt))

        def pb(name, shape):
            return ctx.enter_context(nc.psum_tensor(name, shape, F32))

        def sem(name):
            return ctx.enter_context(nc.semaphore(name))

        y = sb("y", [P, N])
        w_sel = sb("w_sel", [P, B, D])
        cat_bc = sb("cat_bc", [C, B], I32)
        cat_f = sb("cat_f", [C, B])
        onehot = sb("onehot", [C, B])
        prm = sb("prm", [P, params.shape[1]])
        idle = sb("idle", [P, HALF], BF16)
        act_bias = sb("act_bias", [P, E, J])
        bias_now = sb("bias_now", [P, 2, J])
        h = sb("h", [P, N])
        h_hi = sb("h_hi", [P, N], F32R)
        h_lo = sb("h_lo", [P, N], F32R)
        gu_raw = sb("gu_raw", [P, 2, I2])
        gu_hi = [sb(f"gu_hi{i}", [P, I2], F32R) for i in range(2)]
        gu_lo = [sb(f"gu_lo{i}", [P, I2], F32R) for i in range(2)]
        dn = [sb(f"dn{i}", [P, KT * D]) for i in range(2)]
        gate = sb("gate", [P, 2, HALF])
        up = sb("up", [P, 2, HALF])
        z = sb("z", [P, 2, Q, HALF])
        scaled = sb("scaled", [P, NH, HALF])
        lg = sb("lg", [P, NH, TH, E])
        gap = sb("gap", [P, TH, E, E])
        before = sb("before", [P, TH, E, E])
        rank = sb("rank", [P, TH, E])
        top = sb("top", [P, TH])
        shifted = sb("shifted", [P, NH, TH, E])
        minus_one = sb("minus_one", [P, 1])
        table_probe = sb("table_probe", [P, 1])
        silu_s = sb("silu_s", [P, NH, TH, E])
        rest = sb("rest", [P, TH, E])
        inv_rest = sb("inv_rest", [P, TH, E])
        expd = sb("expd", [P, TH, E])
        kept = sb("kept", [P, TH, E])
        denom = sb("denom", [P, TH])
        rdenom = sb("rdenom", [P, TH])
        comb = sb("comb", [P, NH, TH, E])
        comb_t = sb("comb_t", [E, N])
        comb_bc = sb("comb_bc", [P, E, N])

        gate_ps = pb("gate_ps", [P, 2, HALF])
        up_ps = pb("up_ps", [P, 2, HALF])
        down_ps = pb("down_ps", [P, NH, HALF])
        misc_ps = pb("misc_ps", [P, 2, HALF])
        lg_ps = misc_ps[:, 0, 0:TH * E].rearrange("p (t e) -> p t e", e=E)

        cuts = [0]
        for width in (E, E * J, E, E, D, P, E * E, 1):
            cuts.append(cuts[-1] + width)
        router_w, gub, dnb, rb, cond_b, ident, least_gap, row_no = (
            prm[:, a:b] for a, b in zip(cuts, cuts[1:]))
        gub = gub.rearrange("p (e j) -> p e j", j=J)
        cond_b = cond_b[0:C, :]
        least_gap = least_gap.rearrange("p (e j) -> p e j", e=E)
        row_no = row_no[0:C, :]

        x_loaded = [sem(f"x_loaded{i}") for i in range(NH)]
        w_loaded = [sem(f"w_loaded{i}") for i in range(GROUPS)]
        w_loaded_pool = [sem(f"w_loaded_pool{i}") for i in range(GROUPS)]
        prm_loaded = sem("prm_loaded")
        cat_loaded = sem("cat_loaded")
        gu_loaded = [sem(f"gu_loaded{i}") for i in range(2)]
        dn_loaded = [sem(f"dn_loaded{i}") for i in range(2)]
        comb_loaded = [[sem(f"comb_loaded{half}_{i}") for i in range(2)] for half in range(NH)]
        out_stored = sem("out_stored")
        idle_ready = sem("idle_ready")
        minus_one_ready = sem("minus_one_ready")
        onehot_ready = sem("onehot_ready")
        biases_ready = sem("biases_ready")
        hps_ready = sem("hps_ready")
        hi_ready = sem("hi_ready")
        lo_ready = sem("lo_ready")
        logits_ready = sem("logits_ready")
        shifted_ready = sem("shifted_ready")
        silu_ready = sem("silu_ready")
        rank_ready = sem("rank_ready")
        comb_ready = sem("comb_ready")
        combt_ready = sem("combt_ready")
        combt_copied = sem("combt_copied")
        bias_placed = sem("bias_placed")
        w_hi_ready = sem("w_hi_ready")
        w_lo_ready = sem("w_lo_ready")
        gate_ready = sem("gate_ready")
        up_ready = sem("up_ready")
        gate_done = sem("gate_done")
        up_done = sem("up_done")
        up_clamped = sem("up_clamped")
        z_done = sem("z_done")
        down_step = sem("down_step")
        down_read = [sem(f"down_read{half}") for half in range(NH)]
        y_added = sem("y_added")
        dve_step = sem("dve_step")

        block = ctx.enter_context(nc.Block())

        def batches(half, queue, g):
            first = half * BH + sum(sum(SHARE[half][other]) for other in QUEUES[:QUEUES.index(queue)])
            counts = SHARE[half][queue]
            return range(first + sum(counts[:g]), first + sum(counts[:g + 1]))

        def load_ids(engine, regs, half, queue):
            first = batches(half, queue, 0)[0]
            count = sum(SHARE[half][queue])
            for i in range(0, count, 4):
                n = min(4, count - i)
                engine.load(regs[i:i + n], cat_ids[0:1, first + i:first + i + n])

        def gather(engine, regs, half, g, queue, loaded):
            first = batches(half, queue, 0)[0]
            for b in batches(half, queue, g):
                c = engine.snap(regs[b - first], min_val=0, max_val=C - 1)
                engine.dma_start(w_sel[:, b:b + 1, :],
                                 cond_w[bass.ds(c, 1), :, :].rearrange("c d k -> d c k")
                                 ).then_inc(loaded[half * GH + g], 16)

        @block.sync
        def _(sp):
            regs = [sp.alloc_register(f"sp_id{i}") for i in range(max(sum(share["sp"]) for share in SHARE))]

            def load_gate_up(e, slot):
                sp.dma_start(gu_raw[:, slot, :],
                             gate_up_w[bass.ds(of(e, 1), 1), :, :].rearrange("e d j -> d (e j)")
                             ).then_inc(gu_loaded[slot], 16)

            def load_down(e, slot):
                sp.dma_start(dn[slot][:, :], down_w[bass.ds(of(e, 1), 1), :, :].rearrange("e p n -> p (e n)")
                             ).then_inc(dn_loaded[slot], 16)

            def load_comb(e, half):
                sl = slice(half * HALF, (half + 1) * HALF)
                sp.dma_start(comb_bc[:, e, sl], comb_t[e:e + 1, sl].unsqueeze(1).to_broadcast([1, P, HALF])
                             ).then_inc(comb_loaded[half][e % 2], 16)

            sp.dma_start(prm[:, :], params).then_inc(prm_loaded, 16)
            for half in range(NH):
                load_ids(sp, regs, half, "sp")
                for g in range(GH):
                    gather(sp, regs, half, g, "sp", w_loaded)
                    if half == 0 and g == 0:
                        load_gate_up(0, 0)
            load_gate_up(1, 1)
            load_down(0, 0)
            load_down(1, 1)
            def reload_gate_up(e, slot):
                sp.wait_ge(w_lo_ready, of(e, 1, -1))
                load_gate_up(e, slot)

            def reload_down(e, slot):
                sp.wait_ge(down_step, of(e, Q, -Q))
                load_down(e, slot)

            reload_gate_up(2, 0)
            reload_gate_up(3, 1)
            for half in range(NH):
                sp.wait_ge(combt_copied, half + 1)
                load_comb(0, half)
                load_comb(1, half)
            for e in range(2, E):
                for half in range(NH):
                    sp.wait_ge(comb_loaded[half][e % 2], 16 * (e // 2))
                    load_comb(e, half)

            with sp.Fori(0, E // 2 - 2) as k:
                for slot in range(2):
                    reload_down((k, 2 + slot), slot)
                    reload_gate_up((k, 4 + slot), slot)
            for slot in range(2):
                reload_down(E - 2 + slot, slot)

            for half in range(NH):
                sp.wait_ge(y_added, NH * (E - 1) + half + 1)
                sp.dma_start(out_t[:, half * HALF:(half + 1) * HALF],
                             y[:, half * HALF:(half + 1) * HALF]).then_inc(out_stored, 16)
            sp.wait_ge(out_stored, 16 * NH)

        def split_hi(act, e, slot):
            act.wait_ge(gu_loaded[slot], of(e, 8, 16 - 8 * slot))
            nc.scalar.copy(gu_hi[slot][:, :], gu_raw[:, slot, :]).then_inc(w_hi_ready, 1)
            nc.scalar.copy(bias_now[:, slot, :], act_bias[:, bass.ds(of(e, 1), 1), :].rearrange("p e j -> p (e j)")
                           ).then_inc(bias_placed, 1)

        @block.scalar
        def _(act):
            regs = [act.alloc_register(f"act_id{i}") for i in range(sum(SHARE[0]["act"]))]
            act.dma_start(y[:, 0:HALF], x_t[:, 0:HALF]).then_inc(x_loaded[0], 16)
            load_ids(act, regs, 0, "act")
            for g in range(GH):
                gather(act, regs, 0, g, "act", w_loaded)
            act.wait_ge(minus_one_ready, 1)
            nc.scalar.activation(table_probe[:, :], minus_one[:, :], ACT.Silu)
            act.dma_start(y[:, HALF:N], x_t[:, HALF:N]).then_inc(x_loaded[1], 16)

            def copy_h(half):
                act.wait_ge(hps_ready, half + 1)
                nc.scalar.copy(h[:, half * HALF:(half + 1) * HALF], down_ps[:, half, :]).then_inc(down_read[half], 1)

            def router_silu(half):
                act.wait_ge(shifted_ready, half + 1)
                nc.scalar.activation(silu_s[:, half], shifted[:, half], ACT.Silu, bias=minus_one[:, 0:1]
                                     ).then_inc(silu_ready, 1)

            def copy_comb(half):
                act.wait_ge(combt_ready, half + 1)
                nc.scalar.copy(comb_t[:, half * HALF:(half + 1) * HALF], misc_ps[0:E, 1 - half, :]
                               ).then_inc(combt_copied, 1)

            def gate_of(e, slot, q):
                if q == 0:
                    act.wait_ge(bias_placed, of(e, 1, 1))
                act.wait_ge(gate_ready, of(e, Q, q + 1))
                if e != 0 or q >= 2:
                    act.wait_ge(z_done, of(e, Q, q - 1))
                nc.scalar.activation(gate[:, q % 2, :], gate_ps[:, q % 2, :], ACT.Silu,
                                     bias=bias_now[:, slot, q % KT:q % KT + 1], scale=ALPHA).then_inc(gate_done, 1)

            def up_of(e, slot, q):
                act.wait_ge(up_ready, of(e, Q, q + 1))
                nc.scalar.activation(up[:, q % 2, :], up_ps[:, q % 2, :], ACT.Identity,
                                     bias=bias_now[:, slot, KT + q % KT:KT + q % KT + 1], scale=1.0 / ALPHA).then_inc(up_done, 1)

            def pair(e, slot, q):
                gate_of(e, slot, q)
                up_of(e, slot, q)

            act.wait_ge(biases_ready, 2)
            split_hi(act, 0, 0)
            copy_h(0)
            pair(0, 0, 0)
            gate_of(0, 0, 1)
            router_silu(0)
            split_hi(act, 1, 1)
            copy_h(1)
            up_of(0, 0, 1)
            copy_comb(0)
            router_silu(1)
            pair(0, 0, 2)
            pair(0, 0, 3)
            copy_comb(1)

            def step(e, slot):
                for q in range(Q):
                    pair(e, slot, q)
                    if q == 1:
                        split_hi(act, after(e, 1), 1 - slot)

            with act.Fori(0, E // 2 - 1) as k:
                step((k, 1), 1)
                step((k, 2), 0)
            for q in range(Q):
                pair(E - 1, 1, q)

        @block.vector
        def _(dve):
            steps = [0]

            def link(ins):
                steps[0] += 1
                ins.then_inc(dve_step, 1)
                dve.wait_ge(dve_step, steps[0])

            def bc(ap):
                return ap.unsqueeze(2).to_broadcast([P, TH, E])

            nc.vector.memset(idle[:, :], 0.0).then_inc(idle_ready, 1)
            nc.vector.memset(minus_one[:, :], -1.0).then_inc(minus_one_ready, 1)
            dve.wait_ge(cat_loaded, 16)
            link(nc.vector.tensor_copy(cat_f[:, :], cat_bc[:, :]))
            dve.wait_ge(prm_loaded, 16)
            nc.vector.tensor_scalar(onehot[:, :], cat_f[:, :], row_no, None, ALU.is_equal).then_inc(onehot_ready, 1)
            nc.vector.tensor_scalar(act_bias[:, :, 0:KT], gub[:, :, 0:KT], ALPHA, None, ALU.mult).then_inc(biases_ready, 1)
            nc.vector.tensor_scalar(act_bias[:, :, KT:J], gub[:, :, KT:J], 1.0, 1.0 / ALPHA, ALU.add, ALU.mult).then_inc(biases_ready, 1)

            def split_lo(e, slot):
                dve.wait_ge(w_hi_ready, of(e, 1, 1))
                nc.vector.tensor_tensor(gu_lo[slot][:, :], gu_raw[:, slot, :], gu_hi[slot][:, :].bitcast(F32),
                                        ALU.subtract).then_inc(w_lo_ready, 1)

            def h_split(half):
                sl = slice(half * HALF, (half + 1) * HALF)
                dve.wait_ge(down_read[half], 1)
                nc.vector.tensor_copy(h_hi[:, sl], h[:, sl]).then_inc(hi_ready, 1)
                dve.wait_ge(hi_ready, half + 1)
                nc.vector.tensor_tensor(h_lo[:, sl], h[:, sl], h_hi[:, sl].bitcast(F32),
                                        ALU.subtract).then_inc(lo_ready, 1)

            def router(half):
                own_lg, s = lg[:, half], shifted[:, half]
                dve.wait_ge(logits_ready, half + 1)
                link(nc.vector.tensor_tensor(own_lg, lg_ps, rb.unsqueeze(1).to_broadcast([P, TH, E]), ALU.add))
                link(nc.vector.tensor_reduce(top[:, :], own_lg, AX_X, ALU.max))
                nc.vector.tensor_tensor(s, own_lg, bc(top[:, :]), ALU.subtract).then_inc(shifted_ready, 1)
                link(nc.vector.tensor_tensor(gap[:, :, :, :], own_lg.unsqueeze(2).to_broadcast([P, TH, E, E]),
                                             own_lg.unsqueeze(3).to_broadcast([P, TH, E, E]), ALU.subtract))
                link(nc.vector.tensor_tensor(before[:, :, :, :], gap[:, :, :, :],
                                             least_gap.unsqueeze(1).to_broadcast([P, TH, E, E]), ALU.is_ge))
                nc.vector.tensor_reduce(rank[:, :, :], before[:, :, :, :], AX_X, ALU.add).then_inc(rank_ready, 1)
                dve.wait_ge(silu_ready, half + 1)
                link(nc.vector.scalar_tensor_tensor(rest[:, :, :], s, -1.0, silu_s[:, half], ALU.add, ALU.subtract))
                link(nc.vector.reciprocal(inv_rest[:, :, :], rest[:, :, :]))
                link(nc.vector.tensor_tensor(expd[:, :, :], silu_s[:, half], inv_rest[:, :, :], ALU.mult))
                dve.wait_ge(rank_ready, half + 1)
                link(nc.vector.scalar_tensor_tensor(kept[:, :, :], rank[:, :, :], float(TOP_K), expd[:, :, :],
                                                    ALU.is_lt, ALU.mult))
                link(nc.vector.tensor_reduce(denom[:, :], kept[:, :, :], AX_X, ALU.add))
                link(nc.vector.reciprocal(rdenom[:, :], denom[:, :]))
                nc.vector.tensor_tensor(comb[:, half], kept[:, :, :], bc(rdenom[:, :]), ALU.mult
                                        ).then_inc(comb_ready, 1)

            def pair(e, slot, q):
                dve.wait_ge(up_done, of(e, Q, q + 1))
                nc.vector.tensor_scalar(up[:, q % 2, :], up[:, q % 2, :], (1.0 - LIMIT) / ALPHA,
                                        (1.0 + LIMIT) / ALPHA, ALU.max, ALU.min).then_inc(up_clamped, 1)
                dve.wait_ge(up_clamped, of(e, Q, q + 1))
                dve.wait_ge(gate_done, of(e, Q, q + 1))
                nc.vector.scalar_tensor_tensor(z[:, slot, q, :], gate[:, q % 2, :], SILU_AT_LIMIT,
                                               up[:, q % 2, :], ALU.min, ALU.mult).then_inc(z_done, 1)

            def add_expert(e, slot, half):
                sl = slice(half * HALF, (half + 1) * HALF)
                dve.wait_ge(comb_loaded[half][slot], of(e, 8, 16 - 8 * slot))
                dve.wait_ge(down_step, of(e, Q, KT * (half + 1)))
                nc.vector.scalar_tensor_tensor(
                    scaled[:, half, :], down_ps[:, half, :], dnb[:, bass.ds(of(e, 1), 1)],
                    comb_bc[:, bass.ds(of(e, 1), 1), sl].rearrange("p e n -> p (e n)"),
                    ALU.add, ALU.mult).then_inc(down_read[half], 1)
                dve.wait_ge(down_read[half], of(e, 1, 2))
                nc.vector.tensor_tensor(y[:, sl], y[:, sl], scaled[:, half, :], ALU.add).then_inc(y_added, 1)

            split_lo(0, 0)
            h_split(0)
            pair(0, 0, 0)
            router(0)
            split_lo(1, 1)
            h_split(1)
            pair(0, 0, 1)
            router(1)
            pair(0, 0, 2)
            pair(0, 0, 3)

            def step(e, slot, last=False):
                for q in range(Q):
                    pair(e, slot, q)
                    if q == 1 and not last:
                        split_lo(after(e, 1), 1 - slot)
                    if q >= Q - NH:
                        add_expert(after(e, -1), 1 - slot, q - (Q - NH))

            with dve.Fori(0, E // 2 - 1) as k:
                step((k, 1), 1)
                step((k, 2), 0)
            step(E - 1, 1, last=True)
            for half in range(NH):
                add_expert(E - 1, 1, half)

        @block.gpsimd
        def _(pool):
            regs = [pool.alloc_register(f"pool_id{i}") for i in range(max(sum(share["pool"]) for share in SHARE))]
            pool.dma_start(cat_bc[:, :], cat_ids.partition_broadcast(C)).then_inc(cat_loaded, 16)
            for half in range(NH):
                load_ids(pool, regs, half, "pool")
                for g in range(GH):
                    gather(pool, regs, half, g, "pool", w_loaded_pool)

        @block.tensor
        def _(pe):
            def stay_warm(ps, count):
                for _ in range(count):
                    nc.tensor.matmul(ps, idle[:, 0:P], idle[:, :], start=True, stop=True)

            def condition(half):
                hots = onehot[:, half * BH:(half + 1) * BH].unsqueeze(2).to_broadcast([C, BH, S])
                nc.tensor.matmul(down_ps[:, half, :], cond_b, hots, start=True, stop=False)
                pe.wait_ge(x_loaded[half], 16)
                for g in range(GH):
                    stay_warm(misc_ps[:, 1, :], FILL[half][g])
                    share = SHARE[half]
                    pe.wait_ge(w_loaded[half * GH + g], 16 * (share["sp"][g] + share["act"][g]))
                    pe.wait_ge(w_loaded_pool[half * GH + g], 16 * share["pool"][g])
                    for queue in QUEUES:
                        for b in batches(half, queue, g):
                            i = b - half * BH
                            last = nc.tensor.matmul(down_ps[:, half, i * S:(i + 1) * S], w_sel[:, b, :],
                                                    y[:, b * S:(b + 1) * S], start=False, stop=(i == BH - 1))
                last.then_inc(hps_ready, 1)

            def logits(half):
                pe.wait_ge(down_read[half], 1)
                if half > 0:
                    pe.wait_ge(shifted_ready, half)
                for t in range(TH):
                    at = half * HALF + t * P
                    last = nc.tensor.matmul(lg_ps[:, t, :], h[:, at:at + P], router_w, start=True, stop=True)
                last.then_inc(logits_ready, 1)

            def transpose_comb(half):
                pe.wait_ge(comb_ready, half + 1)
                for t in range(TH):
                    last = nc.tensor.transpose(misc_ps[0:E, 1 - half, t * P:(t + 1) * P], comb[:, half, t, :], ident)
                last.then_inc(combt_ready, 1)

            def product(ps, e, slot, tile, half):
                js = slice(tile * P, (tile + 1) * P)
                ns = slice(half * HALF, (half + 1) * HALF)
                nc.tensor.matmul(ps, gu_lo[slot][:, js], h_hi[:, ns], start=True, stop=False)
                nc.tensor.matmul(ps, gu_hi[slot][:, js], h_hi[:, ns], start=False, stop=False)
                if isinstance(e, int) and e == 0:
                    pe.wait_ge(lo_ready, half + 1)
                return nc.tensor.matmul(ps, gu_hi[slot][:, js], h_lo[:, ns], start=False, stop=True)

            def gate_of(e, slot, q):
                if e != 0 or q >= 2:
                    pe.wait_ge(gate_done, of(e, Q, q - 1))
                product(gate_ps[:, q % 2, :], e, slot, q % KT, q // KT).then_inc(gate_ready, 1)

            def up_of(e, slot, q):
                if e != 0 or q >= 2:
                    pe.wait_ge(up_done, of(e, Q, q - 1))
                product(up_ps[:, q % 2, :], e, slot, KT + q % KT, q // KT).then_inc(up_ready, 1)

            def down(e, slot, q):
                half, tile = q // KT, q % KT
                if tile == 0:
                    pe.wait_ge(down_read[half], of(e, 1, 1))
                pe.wait_ge(z_done, of(e, Q, q + 1))
                nc.tensor.matmul(down_ps[:, half, :], dn[slot][:, tile * D:(tile + 1) * D], z[:, slot, q, :],
                                 start=(tile == 0), stop=(tile == KT - 1)).then_inc(down_step, 1)

            def weights_ready(e):
                pe.wait_ge(w_lo_ready, of(e, 1, 1))

            pe.wait_ge(idle_ready, 1)
            stay_warm(misc_ps[:, 1, :], WARM_UP)
            pe.wait_ge(prm_loaded, 16)
            pe.wait_ge(onehot_ready, 1)
            condition(0)
            stay_warm(misc_ps[:, 1, :], WHILE_SPLIT)
            weights_ready(0)
            pe.wait_ge(hi_ready, 1)
            gate_of(0, 0, 0)
            up_of(0, 0, 0)
            logits(0)
            gate_of(0, 0, 1)
            condition(1)
            up_of(0, 0, 1)
            transpose_comb(0)
            logits(1)
            pe.wait_ge(hi_ready, 2)
            for q in range(2, Q):
                gate_of(0, 0, q)
                up_of(0, 0, q)

            def products(e, slot, q):
                if q == 0:
                    weights_ready(e)
                gate_of(e, slot, q)
                up_of(e, slot, q)
                if q == 0:
                    pe.wait_ge(dn_loaded[1 - slot], of(after(e, -1), 8, 16 - 8 * (1 - slot)))
                down(after(e, -1), 1 - slot, q)

            products(1, 1, 0)
            transpose_comb(1)
            with pe.Fori(0, E // 2 - 1) as k:
                for slot in (1, 0):
                    e = (k, 2 - slot)
                    for q in range(1, Q):
                        products(e, slot, q)
                    products(after(e, 1), 1 - slot, 0)
            for q in range(1, Q):
                products(E - 1, 1, q)
            pe.wait_ge(dn_loaded[1], 8 * (E - 2) + 16)
            for q in range(Q):
                down(E - 1, 1, q)


def _silu_at_limit():
    import math
    a = ALPHA * LIMIT
    return a / (1.0 + math.exp(-a))


SILU_AT_LIMIT = _silu_at_limit()


def kernel(x, itok_B_0_63, L0_cond_W, L0_cond_b, L0_ffn_router_weight, L0_ffn_router_bias,
           L0_ffn_gate_up_proj, L0_ffn_gate_up_proj_bias, L0_ffn_down_proj, L0_ffn_down_proj_bias):
    import numpy as np
    import concourse.bacc as bacc
    from concourse import mybir as mb
    from concourse.bass_utils import run_bass_kernel_spmd

    x = np.asarray(x)
    bsz, s, d = x.shape
    n = bsz * s
    gu = np.asarray(L0_ffn_gate_up_proj)
    dnw = np.asarray(L0_ffn_down_proj)
    e, i2, _ = gu.shape
    kt = i2 // 2 // P
    gub = np.asarray(L0_ffn_gate_up_proj_bias).reshape(e, 2 * kt, P).transpose(2, 0, 1).reshape(P, e * 2 * kt)
    cond_b = np.zeros((P, d), np.float32)
    cond_b[:L0_cond_b.shape[0]] = np.asarray(L0_cond_b)
    least_gap = np.where(np.tril(np.ones((e, e), bool), -1), 0.0, np.finfo(np.float32).tiny).astype(np.float32)
    arrays = {
        "x_t": x.reshape(n, d).T,
        "cat_ids": np.asarray(itok_B_0_63).reshape(1, bsz),
        "cond_w": np.asarray(L0_cond_W),
        "params": np.concatenate([
            np.asarray(L0_ffn_router_weight).T, gub, np.asarray(L0_ffn_down_proj_bias).T,
            np.broadcast_to(np.asarray(L0_ffn_router_bias).reshape(1, e), (P, e)), cond_b,
            np.eye(P, dtype=np.float32), np.broadcast_to(least_gap.reshape(1, e * e), (P, e * e)),
            np.arange(P, dtype=np.float32).reshape(P, 1)], axis=1),
        "gate_up_w": gu.transpose(0, 2, 1),
        "down_w": dnw.reshape(e, d, kt, P).transpose(0, 3, 2, 1).reshape(e, P, kt * d),
    }
    arrays = {k: np.ascontiguousarray(v) for k, v in arrays.items()}
    nc = bacc.Bacc("TRN2", target_bir_lowering=False, num_devices=1)
    args = [nc.dram_tensor(k, a.shape, mb.dt.from_np(a.dtype), kind="ExternalInput").ap() for k, a in arrays.items()]
    args.append(nc.dram_tensor("out_t", (d, n), mb.dt.float32, kind="ExternalOutput").ap())
    adaln_moe_ffn_kernel(nc, *args)
    got = run_bass_kernel_spmd(nc, [arrays], core_ids=[0]).results[0]["out_t"]
    return np.ascontiguousarray(np.asarray(got).T).reshape(bsz, s, d)
```

```python
import concourse.bass as bass
from concourse import mybir
from contextlib import ExitStack

F32 = mybir.dt.float32
F32R = mybir.dt.float32r
BF16 = mybir.dt.bfloat16
I32 = mybir.dt.int32
ALU = mybir.AluOpType
ACT = mybir.ActivationFunctionType
AX_X = mybir.AxisListType.X

P = 128
ALPHA = 1.702
LIMIT = 7.0
TOP_K = 4
WARM_UP = 12
PE_AHEAD = 2
ACT_AHEAD = 1


def adaln_moe_ffn_kernel(
    nc: bass.Bass,
    x_t: bass.AP,
    cat_ids: bass.AP,
    cond_w: bass.AP,
    params: bass.AP,
    gate_up_w: bass.AP,
    down_w: bass.AP,
    out_t: bass.AP,
):
    D, N = x_t.shape
    C = cond_w.shape[0]
    B = cat_ids.shape[1]
    S = N // B
    E = gate_up_w.shape[0]
    I2 = gate_up_w.shape[2]
    KT = I2 // 2 // P
    J = 2 * KT
    HALF = 512
    NH = N // HALF
    BH = HALF // S
    TH = HALF // P
    Q = NH * KT
    QUARTER = HALF // 2
    QUARTERS = N // QUARTER
    BQ = QUARTER // S
    SHARE = [{"sp": 4, "act": 2, "pool": 2}, {"sp": 2, "act": 2, "pool": 4},
             {"sp": 4, "act": 0, "pool": 4}, {"sp": 4, "act": 0, "pool": 4}]
    QUEUES = ("sp", "act", "pool")
    GROUPS = 2
    PIECES = [(0, HALF), (HALF, QUARTER), (HALF + QUARTER, QUARTER)]
    assert D == P and N == NH * HALF and NH == 2 and KT == 2 and E % 2 == 0 and E >= 6 and QUARTERS == len(SHARE)

    def of(e, times, plus=0):
        if isinstance(e, int):
            return times * e + plus
        k, c = e
        return k * (2 * times) + (times * c + plus)

    def after(e, more):
        return e + more if isinstance(e, int) else (e[0], e[1] + more)

    with ExitStack() as ctx:
        def sb(name, shape, dt=F32):
            return ctx.enter_context(nc.sbuf_tensor(name, shape, dt))

        def pb(name, shape):
            return ctx.enter_context(nc.psum_tensor(name, shape, F32))

        def sem(name):
            return ctx.enter_context(nc.semaphore(name))

        y = sb("y", [P, N])
        w_sel = sb("w_sel", [P, B, D])
        cat_bc = sb("cat_bc", [C, B], I32)
        cat_f = sb("cat_f", [C, B])
        onehot = sb("onehot", [C, B])
        prm = sb("prm", [P, params.shape[1]])
        idle = sb("idle", [P, HALF], BF16)
        act_bias = sb("act_bias", [P, E, J])
        bias_now = sb("bias_now", [P, 2, J])
        h = sb("h", [P, N])
        h_hi = sb("h_hi", [P, N], F32R)
        h_lo = sb("h_lo", [P, N], F32R)
        gu_raw = sb("gu_raw", [P, 2, I2])
        gu_hi = [sb(f"gu_hi{i}", [P, I2], F32R) for i in range(2)]
        gu_lo = [sb(f"gu_lo{i}", [P, I2], F32R) for i in range(2)]
        dn = [sb(f"dn{i}", [P, KT * D]) for i in range(2)]
        dn_hi = [sb(f"dn_hi{i}", [P, D], F32R) for i in range(2)]
        dn_lo = [sb(f"dn_lo{i}", [P, D], F32R) for i in range(2)]
        gate = sb("gate", [P, 2, HALF])
        up = sb("up", [P, 2, HALF])
        z = sb("z", [P, 2, Q, HALF])
        z_hi = [sb(f"z_hi{half}", [P, HALF], F32R) for half in range(NH)]
        z_lo = [sb(f"z_lo{half}", [P, HALF], F32R) for half in range(NH)]
        scaled = sb("scaled", [P, NH, HALF])
        lg = sb("lg", [P, NH, TH, E])
        gap = sb("gap", [P, TH, E, E])
        before = sb("before", [P, TH, E, E])
        rank = sb("rank", [P, TH, E])
        top = sb("top", [P, TH])
        shifted = sb("shifted", [P, NH, TH, E])
        minus_one = sb("minus_one", [P, 1])
        table_probe = sb("table_probe", [P, 1])
        silu_s = sb("silu_s", [P, NH, TH, E])
        rest = sb("rest", [P, TH, E])
        inv_rest = sb("inv_rest", [P, TH, E])
        expd = sb("expd", [P, TH, E])
        kept = sb("kept", [P, TH, E])
        denom = sb("denom", [P, TH])
        rdenom = sb("rdenom", [P, TH])
        comb = sb("comb", [P, NH, TH, E])
        comb_t = sb("comb_t", [E, N])
        comb_bc = sb("comb_bc", [P, E, N])

        gate_ps = pb("gate_ps", [P, 2, HALF])
        up_ps = pb("up_ps", [P, 2, HALF])
        down_ps = pb("down_ps", [P, NH, HALF])
        misc_ps = pb("misc_ps", [P, 2, HALF])
        last_ps = [down_ps[:, NH - 1, 0:QUARTER], misc_ps[:, 0, 0:QUARTER]]
        lg_ps = misc_ps[:, 0, 0:TH * E].rearrange("p (t e) -> p t e", e=E)

        cuts = [0]
        for width in (E, E * J, E, E, D, P, E * E, 1):
            cuts.append(cuts[-1] + width)
        router_w, gub, dnb, rb, cond_b, ident, least_gap, row_no = (
            prm[:, a:b] for a, b in zip(cuts, cuts[1:]))
        gub = gub.rearrange("p (e j) -> p e j", j=J)
        cond_b = cond_b[0:C, :]
        least_gap = least_gap.rearrange("p (e j) -> p e j", e=E)
        row_no = row_no[0:C, :]

        x_loaded = [sem(f"x_loaded{i}") for i in range(NH)]
        w_loaded = [sem(f"w_loaded{i}") for i in range(QUARTERS * GROUPS)]
        w_loaded_pool = [sem(f"w_loaded_pool{i}") for i in range(QUARTERS * GROUPS)]
        prm_loaded = sem("prm_loaded")
        cat_loaded = sem("cat_loaded")
        gu_loaded = [sem(f"gu_loaded{i}") for i in range(2)]
        dn_loaded = [sem(f"dn_loaded{i}") for i in range(2)]
        comb_loaded = [[sem(f"comb_loaded{half}_{i}") for i in range(2)] for half in range(NH)]
        out_stored = sem("out_stored")
        idle_ready = sem("idle_ready")
        minus_one_ready = sem("minus_one_ready")
        onehot_ready = sem("onehot_ready")
        biases_ready = sem("biases_ready")
        hps_ready = sem("hps_ready")
        hi_ready = sem("hi_ready")
        lo_ready = sem("lo_ready")
        logits_ready = sem("logits_ready")
        shifted_ready = sem("shifted_ready")
        silu_ready = sem("silu_ready")
        rank_ready = sem("rank_ready")
        comb_ready = sem("comb_ready")
        combt_ready = sem("combt_ready")
        combt_copied = sem("combt_copied")
        bias_placed = sem("bias_placed")
        w_hi_ready = sem("w_hi_ready")
        w_lo_ready = sem("w_lo_ready")
        dn_hi_ready = sem("dn_hi_ready")
        dn_lo_ready = sem("dn_lo_ready")
        z_hi_ready = sem("z_hi_ready")
        z_lo_ready = sem("z_lo_ready")
        gate_ready = sem("gate_ready")
        up_ready = sem("up_ready")
        gate_done = sem("gate_done")
        up_done = sem("up_done")
        up_clamped = sem("up_clamped")
        z_done = sem("z_done")
        down_step = sem("down_step")
        down_read = [sem(f"down_read{half}") for half in range(NH)]
        y_added = sem("y_added")
        pool_added = sem("pool_added")
        dve_step = sem("dve_step")

        block = ctx.enter_context(nc.Block())

        def batches(t, queue, g):
            first = t * BQ + sum(SHARE[t][other] for other in QUEUES[:QUEUES.index(queue)])
            count = SHARE[t][queue] // GROUPS
            return range(first + g * count, first + (g + 1) * count)

        def id_registers(engine, queue):
            return [[engine.alloc_register(f"{queue}_id{t}_{i}") for i in range(SHARE[t][queue])]
                    for t in range(QUARTERS)]

        def load_ids(engine, regs, t, queue):
            first, count = batches(t, queue, 0)[0], SHARE[t][queue]
            for i in range(0, count, 4):
                engine.load(regs[t][i:i + 4], cat_ids[0:1, first + i:first + min(i + 4, count)])

        def gather(engine, regs, t, queue, loaded):
            for g in range(GROUPS):
                for b in batches(t, queue, g):
                    c = engine.snap(regs[t][b - batches(t, queue, 0)[0]], min_val=0, max_val=C - 1)
                    engine.dma_start(w_sel[:, b:b + 1, :],
                                     cond_w[bass.ds(c, 1), :, :].rearrange("c d k -> d c k")
                                     ).then_inc(loaded[t * GROUPS + g], 16)

        def load_down(engine, e, slot):
            engine.dma_start(dn[slot][:, :], down_w[bass.ds(of(e, 1), 1), :, :].rearrange("e p n -> p (e n)")
                             ).then_inc(dn_loaded[slot], 16)

        def add(engine, half, first=0, count=HALF):
            cols = slice(half * HALF + first, half * HALF + first + count)
            return engine.tensor_tensor(y[:, cols], y[:, cols], scaled[:, half, first:first + count], ALU.add)

        def store(engine, piece):
            first, count = PIECES[piece]
            if piece == 0:
                engine.wait_ge(pool_added, 3)
            else:
                engine.wait_ge(y_added, NH * (E - 2) + piece)
            engine.dma_start(out_t[:, first:first + count], y[:, first:first + count]).then_inc(out_stored, 16)

        @block.sync
        def _(sp):
            regs = id_registers(sp, "sp")

            def load_gate_up(e, slot):
                sp.dma_start(gu_raw[:, slot, :],
                             gate_up_w[bass.ds(of(e, 1), 1), :, :].rearrange("e d j -> d (e j)")
                             ).then_inc(gu_loaded[slot], 16)

            def load_comb(e, half):
                sl = slice(half * HALF, (half + 1) * HALF)
                sp.dma_start(comb_bc[:, e, sl], comb_t[e:e + 1, sl].unsqueeze(1).to_broadcast([1, P, HALF])
                             ).then_inc(comb_loaded[half][e % 2], 16)

            sp.dma_start(prm[:, :], params).then_inc(prm_loaded, 16)
            load_ids(sp, regs, 0, "sp")
            load_ids(sp, regs, 1, "sp")
            gather(sp, regs, 0, "sp", w_loaded)
            load_gate_up(0, 0)
            gather(sp, regs, 1, "sp", w_loaded)
            load_ids(sp, regs, 2, "sp")
            load_ids(sp, regs, 3, "sp")
            gather(sp, regs, 2, "sp", w_loaded)
            gather(sp, regs, 3, "sp", w_loaded)
            load_gate_up(1, 1)
            load_down(sp, 0, 0)
            load_down(sp, 1, 1)

            def reload_gate_up(e):
                sp.wait_ge(w_lo_ready, e - 1)
                load_gate_up(e, e % 2)

            reload_gate_up(2)
            reload_gate_up(3)
            for half in range(NH):
                sp.wait_ge(combt_copied, half + 1)
                load_comb(0, half)
                load_comb(1, half)
            reload_gate_up(4)
            for e in range(2, E):
                for half in range(NH):
                    sp.wait_ge(comb_loaded[half][e % 2], 16 * (e // 2))
                    load_comb(e, half)
            for e in range(5, E):
                reload_gate_up(e)

            store(sp, 0)
            store(sp, 2)
            sp.wait_ge(out_stored, 16 * len(PIECES))

        def split_hi(act, e, slot):
            act.wait_ge(gu_loaded[slot], of(e, 8, 16 - 8 * slot))
            nc.scalar.copy(gu_hi[slot][:, :], gu_raw[:, slot, :]).then_inc(w_hi_ready, 1)
            nc.scalar.copy(bias_now[:, slot, :], act_bias[:, bass.ds(of(e, 1), 1), :].rearrange("p e j -> p (e j)")
                           ).then_inc(bias_placed, 1)

        @block.scalar
        def _(act):
            regs = id_registers(act, "act")
            act.dma_start(y[:, 0:HALF], x_t[:, 0:HALF]).then_inc(x_loaded[0], 16)
            load_ids(act, regs, 0, "act")
            gather(act, regs, 0, "act", w_loaded)
            load_ids(act, regs, 1, "act")
            gather(act, regs, 1, "act", w_loaded)
            act.wait_ge(minus_one_ready, 1)
            nc.scalar.activation(table_probe[:, :], minus_one[:, :], ACT.Silu)
            act.dma_start(y[:, HALF:N], x_t[:, HALF:N]).then_inc(x_loaded[1], 16)

            def copy_h(t):
                sl = slice(t * QUARTER, (t + 1) * QUARTER)
                act.wait_ge(hps_ready, t + 1)
                nc.scalar.copy(h_hi[:, sl], down_ps[:, t % 2, 0:QUARTER]).then_inc(hi_ready, 1)
                nc.scalar.copy(h[:, sl], down_ps[:, t % 2, 0:QUARTER]).then_inc(down_read[t % 2], 1)

            def down_upper(e, slot):
                act.wait_ge(dn_loaded[slot], of(e, 8, 16 - 8 * slot))
                nc.scalar.copy(dn_hi[slot][:, :], dn[slot][:, (KT - 1) * D:KT * D]).then_inc(dn_hi_ready, 1)

            def z_upper(e, slot, half):
                q = half * KT + KT - 1
                act.wait_ge(z_done, of(e, Q, q + 1))
                if e != 0:
                    act.wait_ge(down_step, of(e, Q, q + 1 - Q))
                nc.scalar.copy(z_hi[half][:, :], z[:, slot, q, :]).then_inc(z_hi_ready, 1)

            def router_silu(half):
                act.wait_ge(shifted_ready, half + 1)
                nc.scalar.activation(silu_s[:, half], shifted[:, half], ACT.Silu, bias=minus_one[:, 0:1]
                                     ).then_inc(silu_ready, 1)

            def copy_comb(half):
                act.wait_ge(combt_ready, half + 1)
                nc.scalar.copy(comb_t[:, half * HALF:(half + 1) * HALF], misc_ps[0:E, 1 - half, :]
                               ).then_inc(combt_copied, 1)

            def gate_of(e, slot, q):
                if q == 0:
                    act.wait_ge(bias_placed, of(e, 1, 1))
                act.wait_ge(gate_ready, of(e, Q, q + 1))
                if e != 0 or q >= 2:
                    act.wait_ge(z_done, of(e, Q, q - 1))
                nc.scalar.activation(gate[:, q % 2, :], gate_ps[:, q % 2, :], ACT.Silu,
                                     bias=bias_now[:, slot, q % KT:q % KT + 1], scale=ALPHA).then_inc(gate_done, 1)

            def up_of(e, slot, q):
                act.wait_ge(up_ready, of(e, Q, q + 1))
                nc.scalar.activation(up[:, q % 2, :], up_ps[:, q % 2, :], ACT.Identity,
                                     bias=bias_now[:, slot, KT + q % KT:KT + q % KT + 1], scale=1.0 / ALPHA).then_inc(up_done, 1)

            def pair(e, slot, q):
                gate_of(e, slot, q)
                up_of(e, slot, q)

            act.wait_ge(biases_ready, 2)
            split_hi(act, 0, 0)
            copy_h(0)
            copy_h(1)
            pair(0, 0, 0)
            pair(0, 0, 1)
            router_silu(0)
            split_hi(act, 1, 1)
            copy_h(2)
            copy_h(3)
            copy_comb(0)
            pair(0, 0, 2)
            router_silu(1)
            pair(0, 0, 3)
            down_upper(0, 0)

            def pairs(e, slot, qs):
                for q in qs:
                    pair(e, slot, q)
                    if q == 0:
                        act.wait_ge(down_step, of(e, Q, -Q))
                        load_down(act, e, slot)
                    if q == 1:
                        split_hi(act, after(e, 1), 1 - slot)
                        z_upper(after(e, -1), 1 - slot, 1)
                    if q == 2:
                        down_upper(e, slot)
                    if q == 3:
                        z_upper(e, slot, 0)

            copy_comb(1)
            for q in range(ACT_AHEAD):
                pair(1, 1, q)
            with act.Fori(0, E // 2 - 1) as k:
                for slot in (1, 0):
                    e = (k, 2 - slot)
                    pairs(e, slot, range(ACT_AHEAD, Q))
                    pairs(after(e, 1), 1 - slot, range(ACT_AHEAD))
            for q in range(ACT_AHEAD, Q):
                pair(E - 1, 1, q)
            store(act, 1)

        @block.vector
        def _(dve):
            steps = [0]

            def link(ins):
                steps[0] += 1
                ins.then_inc(dve_step, 1)
                dve.wait_ge(dve_step, steps[0])

            def bc(ap):
                return ap.unsqueeze(2).to_broadcast([P, TH, E])

            nc.vector.memset(idle[:, :], 0.0).then_inc(idle_ready, 1)
            nc.vector.memset(minus_one[:, :], -1.0).then_inc(minus_one_ready, 1)
            dve.wait_ge(cat_loaded, 16)
            link(nc.vector.tensor_copy(cat_f[:, :], cat_bc[:, :]))
            dve.wait_ge(prm_loaded, 16)
            nc.vector.tensor_scalar(onehot[:, :], cat_f[:, :], row_no, None, ALU.is_equal).then_inc(onehot_ready, 1)
            nc.vector.tensor_scalar(act_bias[:, :, 0:KT], gub[:, :, 0:KT], ALPHA, None, ALU.mult).then_inc(biases_ready, 1)
            nc.vector.tensor_scalar(act_bias[:, :, KT:J], gub[:, :, KT:J], 1.0, 1.0 / ALPHA, ALU.add, ALU.mult).then_inc(biases_ready, 1)

            def split_lo(e, slot):
                dve.wait_ge(w_hi_ready, of(e, 1, 1))
                nc.vector.tensor_tensor(gu_lo[slot][:, :], gu_raw[:, slot, :], gu_hi[slot][:, :].bitcast(F32),
                                        ALU.subtract).then_inc(w_lo_ready, 1)

            def down_lower(e, slot):
                dve.wait_ge(dn_hi_ready, of(e, 1, 1))
                nc.vector.tensor_tensor(dn_lo[slot][:, :], dn[slot][:, (KT - 1) * D:KT * D],
                                        dn_hi[slot][:, :].bitcast(F32), ALU.subtract).then_inc(dn_lo_ready, 1)

            def h_rest(t):
                sl = slice(t * QUARTER, (t + 1) * QUARTER)
                dve.wait_ge(hi_ready, t + 1)
                dve.wait_ge(down_read[t % 2], t // 2 + 1)
                nc.vector.tensor_tensor(h_lo[:, sl], h[:, sl], h_hi[:, sl].bitcast(F32),
                                        ALU.subtract).then_inc(lo_ready, 1)

            def router(half):
                own_lg, s = lg[:, half], shifted[:, half]
                dve.wait_ge(logits_ready, half + 1)
                link(nc.vector.tensor_tensor(own_lg, lg_ps, rb.unsqueeze(1).to_broadcast([P, TH, E]), ALU.add))
                link(nc.vector.tensor_reduce(top[:, :], own_lg, AX_X, ALU.max))
                nc.vector.tensor_tensor(s, own_lg, bc(top[:, :]), ALU.subtract).then_inc(shifted_ready, 1)
                link(nc.vector.tensor_tensor(gap[:, :, :, :], own_lg.unsqueeze(2).to_broadcast([P, TH, E, E]),
                                             own_lg.unsqueeze(3).to_broadcast([P, TH, E, E]), ALU.subtract))
                link(nc.vector.tensor_tensor(before[:, :, :, :], gap[:, :, :, :],
                                             least_gap.unsqueeze(1).to_broadcast([P, TH, E, E]), ALU.is_ge))
                nc.vector.tensor_reduce(rank[:, :, :], before[:, :, :, :], AX_X, ALU.add).then_inc(rank_ready, 1)
                dve.wait_ge(silu_ready, half + 1)
                link(nc.vector.scalar_tensor_tensor(rest[:, :, :], s, -1.0, silu_s[:, half], ALU.add, ALU.subtract))
                link(nc.vector.reciprocal(inv_rest[:, :, :], rest[:, :, :]))
                link(nc.vector.tensor_tensor(expd[:, :, :], silu_s[:, half], inv_rest[:, :, :], ALU.mult))
                dve.wait_ge(rank_ready, half + 1)
                link(nc.vector.scalar_tensor_tensor(kept[:, :, :], rank[:, :, :], float(TOP_K), expd[:, :, :],
                                                    ALU.is_lt, ALU.mult))
                link(nc.vector.tensor_reduce(denom[:, :], kept[:, :, :], AX_X, ALU.add))
                link(nc.vector.reciprocal(rdenom[:, :], denom[:, :]))
                nc.vector.tensor_tensor(comb[:, half], kept[:, :, :], bc(rdenom[:, :]), ALU.mult
                                        ).then_inc(comb_ready, 1)

            def clamp(e, q):
                dve.wait_ge(up_done, of(e, Q, q + 1))
                nc.vector.tensor_scalar(up[:, q % 2, :], up[:, q % 2, :], (1.0 - LIMIT) / ALPHA,
                                        (1.0 + LIMIT) / ALPHA, ALU.max, ALU.min).then_inc(up_clamped, 1)

            def activate(e, slot, q):
                dve.wait_ge(gate_done, of(e, Q, q + 1))
                dve.wait_ge(up_clamped, of(e, Q, q + 1))
                nc.vector.scalar_tensor_tensor(z[:, slot, q, :], gate[:, q % 2, :], SILU_AT_LIMIT,
                                               up[:, q % 2, :], ALU.min, ALU.mult).then_inc(z_done, 1)

            def pair(e, slot, q):
                clamp(e, q)
                activate(e, slot, q)

            def z_lower(e, slot, half):
                dve.wait_ge(z_hi_ready, of(e, NH, half))
                nc.vector.tensor_tensor(z_lo[half][:, :], z[:, slot, half * KT + KT - 1, :],
                                        z_hi[half][:, :].bitcast(F32), ALU.subtract).then_inc(z_lo_ready, 1)

            def weight(e, half, first=0, count=HALF):
                cols = slice(half * HALF + first, half * HALF + first + count)
                return nc.vector.scalar_tensor_tensor(
                    scaled[:, half, first:first + count],
                    down_ps[:, half, :] if count == HALF else last_ps[first // count],
                    dnb[:, bass.ds(of(e, 1), 1)],
                    comb_bc[:, bass.ds(of(e, 1), 1), cols].rearrange("p e n -> p (e n)"),
                    ALU.add, ALU.mult)

            def weight_half(e, slot, half):
                dve.wait_ge(comb_loaded[half][slot], of(e, 8, 16 - 8 * slot))
                dve.wait_ge(down_step, of(e, Q, KT * (half + 1)))
                weight(e, half).then_inc(down_read[half], 1)

            def add_half(e, half):
                dve.wait_ge(down_read[half], of(e, 1, 3))
                add(nc.vector, half).then_inc(y_added, 1)

            split_lo(0, 0)
            h_rest(0)
            h_rest(1)
            pair(0, 0, 0)
            router(0)
            h_rest(2)
            h_rest(3)
            pair(0, 0, 1)
            split_lo(1, 1)
            router(1)
            pair(0, 0, 2)
            pair(0, 0, 3)
            down_lower(0, 0)

            def step(e, slot):
                before, its_slot = after(e, -1), 1 - slot
                clamp(e, 0)
                activate(e, slot, 0)
                clamp(e, 1)
                z_lower(before, its_slot, 1)
                activate(e, slot, 1)
                clamp(e, 2)
                weight_half(before, its_slot, 0)
                activate(e, slot, 2)
                add_half(before, 0)
                clamp(e, 3)
                z_lower(e, slot, 0)
                down_lower(e, slot)
                activate(e, slot, 3)
                weight_half(before, its_slot, 1)
                add_half(before, 1)

            with dve.Fori(0, E // 2 - 1) as k:
                step((k, 1), 1)
                step((k, 2), 0)
            clamp(E - 1, 0)
            activate(E - 1, 1, 0)
            clamp(E - 1, 1)
            activate(E - 1, 1, 1)
            weight_half(E - 2, 0, 0)
            clamp(E - 1, 2)
            activate(E - 1, 1, 2)
            clamp(E - 1, 3)
            weight_half(E - 2, 0, 1)
            activate(E - 1, 1, 3)
            dve.wait_ge(pool_added, 1)
            weight_half(E - 1, 1, 0)
            dve.wait_ge(comb_loaded[1][1], 16 * (E // 2))
            dve.wait_ge(pool_added, 2)
            for piece in range(2):
                dve.wait_ge(down_step, (E - 1) * Q + KT + 1 + piece)
                weight(E - 1, 1, piece * QUARTER, QUARTER).then_inc(down_read[1], 1)
                dve.wait_ge(down_read[1], E + 2 + piece)
                add(nc.vector, 1, piece * QUARTER, QUARTER).then_inc(y_added, 1)

        @block.gpsimd
        def _(pool):
            regs = id_registers(pool, "pool")
            pool.dma_start(cat_bc[:, :], cat_ids.partition_broadcast(C)).then_inc(cat_loaded, 16)
            for t in range(QUARTERS):
                load_ids(pool, regs, t, "pool")
                gather(pool, regs, t, "pool", w_loaded_pool)

            def split_lo(e, slot):
                pool.wait_ge(w_hi_ready, of(e, 1, 1))
                nc.gpsimd.tensor_tensor(gu_lo[slot][:, :], gu_raw[:, slot, :], gu_hi[slot][:, :].bitcast(F32),
                                        ALU.subtract).then_inc(w_lo_ready, 1)

            with pool.Fori(0, E // 2 - 1) as k:
                for slot in (1, 0):
                    e = (k, 2 - slot)
                    split_lo(after(e, 1), 1 - slot)
            pool.wait_ge(y_added, NH * (E - 2))
            for e, half in ((E - 2, 0), (E - 2, 1), (E - 1, 0)):
                pool.wait_ge(down_read[half], e + 3)
                if e == E - 1:
                    pool.wait_ge(pool_added, 2)
                add(nc.gpsimd, half).then_inc(pool_added, 1)

        @block.tensor
        def _(pe):
            def stay_warm(count):
                for _ in range(count):
                    nc.tensor.matmul(misc_ps[:, 1, :], idle[:, 0:P], idle[:, :], start=True, stop=True)

            def condition_bias(t):
                if t >= 2:
                    pe.wait_ge(down_read[t % 2], t // 2)
                hots = onehot[:, t * BQ:(t + 1) * BQ].unsqueeze(2).to_broadcast([C, BQ, S])
                nc.tensor.matmul(down_ps[:, t % 2, 0:QUARTER], cond_b, hots, start=True, stop=False)
                pe.wait_ge(x_loaded[t // 2], 16)

            def condition(t, g):
                pool_count = SHARE[t]["pool"] // GROUPS
                pe.wait_ge(w_loaded[t * GROUPS + g], 16 * (BQ // GROUPS - pool_count))
                pe.wait_ge(w_loaded_pool[t * GROUPS + g], 16 * pool_count)
                for queue in QUEUES:
                    for b in batches(t, queue, g):
                        at = (b - t * BQ) * S
                        last = nc.tensor.matmul(down_ps[:, t % 2, at:at + S], w_sel[:, b, :],
                                                y[:, b * S:(b + 1) * S], start=False, stop=(b == (t + 1) * BQ - 1))
                if g == GROUPS - 1:
                    last.then_inc(hps_ready, 1)

            def logits(t):
                half = t // 2
                if t == 2:
                    pe.wait_ge(shifted_ready, 1)
                pe.wait_ge(down_read[t % 2], half + 1)
                for i in range(QUARTER // P):
                    at = t * QUARTER + i * P
                    last = nc.tensor.matmul(lg_ps[:, (at - half * HALF) // P, :], h[:, at:at + P], router_w,
                                            start=True, stop=True)
                if t % 2 == 1:
                    last.then_inc(logits_ready, 1)

            def transpose_comb(half):
                pe.wait_ge(comb_ready, half + 1)
                for t in range(TH):
                    last = nc.tensor.transpose(misc_ps[0:E, 1 - half, t * P:(t + 1) * P], comb[:, half, t, :], ident)
                last.then_inc(combt_ready, 1)

            def product(ps, slot, tile, first, count, wait_lo=None):
                js = slice(tile * P, (tile + 1) * P)
                ns = slice(first, first + count)
                nc.tensor.matmul(ps, gu_lo[slot][:, js], h_hi[:, ns], start=True, stop=False)
                nc.tensor.matmul(ps, gu_hi[slot][:, js], h_hi[:, ns], start=False, stop=False)
                if wait_lo is not None:
                    pe.wait_ge(lo_ready, wait_lo)
                return nc.tensor.matmul(ps, gu_hi[slot][:, js], h_lo[:, ns], start=False, stop=True)

            def quarter_pair(t, q):
                pe.wait_ge(hi_ready, t + 1)
                cols = slice(t * QUARTER, (t + 1) * QUARTER)
                gate = product(gate_ps[:, q, cols], 0, q, t * QUARTER, QUARTER, t + 1)
                up = product(up_ps[:, q, cols], 0, KT + q, t * QUARTER, QUARTER)
                if t == 1:
                    gate.then_inc(gate_ready, 1)
                    up.then_inc(up_ready, 1)

            def gate_of(e, slot, q, wait_lo=None):
                pe.wait_ge(gate_done, of(e, Q, q - 1))
                product(gate_ps[:, q % 2, :], slot, q % KT, q // KT * HALF, HALF, wait_lo).then_inc(gate_ready, 1)

            def up_of(e, slot, q):
                pe.wait_ge(up_done, of(e, Q, q - 1))
                product(up_ps[:, q % 2, :], slot, KT + q % KT, q // KT * HALF, HALF).then_inc(up_ready, 1)

            def down(e, slot, q, split=True, first=0, count=HALF):
                half, tile = q // KT, q % KT
                if tile == 0:
                    pe.wait_ge(down_read[half], of(e, 1, 2))
                ps = down_ps[:, half, :] if count == HALF else last_ps[first // count]
                if split and tile == KT - 1:
                    pe.wait_ge(dn_lo_ready, of(e, 1, 1))
                    pe.wait_ge(z_lo_ready, of(e, NH, half))
                    nc.tensor.matmul(ps, dn_lo[slot][:, :], z_hi[half][:, :], start=False, stop=False)
                    nc.tensor.matmul(ps, dn_hi[slot][:, :], z_hi[half][:, :], start=False, stop=False)
                    last = nc.tensor.matmul(ps, dn_hi[slot][:, :], z_lo[half][:, :], start=False, stop=True)
                else:
                    pe.wait_ge(z_done, of(e, Q, q + 1))
                    last = nc.tensor.matmul(ps, dn[slot][:, tile * D:(tile + 1) * D],
                                            z[:, slot, q, first:first + count],
                                            start=(tile == 0), stop=(tile == KT - 1))
                if count == HALF or tile == KT - 1:
                    last.then_inc(down_step, 1)

            def weights_ready(e):
                pe.wait_ge(w_lo_ready, of(e, 1, 1))

            pe.wait_ge(idle_ready, 1)
            stay_warm(WARM_UP)
            pe.wait_ge(prm_loaded, 16)
            pe.wait_ge(onehot_ready, 1)
            condition_bias(0)
            stay_warm(2)
            condition(0, 0)
            stay_warm(2)
            condition(0, 1)
            condition_bias(1)
            condition(1, 0)
            weights_ready(0)
            quarter_pair(0, 0)
            condition(1, 1)
            quarter_pair(0, 1)
            logits(0)
            quarter_pair(1, 0)
            logits(1)
            condition_bias(2)
            condition(2, 0)
            quarter_pair(1, 1)
            condition(2, 1)
            condition_bias(3)
            condition(3, 0)
            stay_warm(1)
            condition(3, 1)
            stay_warm(1)
            logits(2)
            transpose_comb(0)
            logits(3)
            pe.wait_ge(hi_ready, QUARTERS)
            for q in range(2, Q):
                gate_of(0, 0, q, QUARTERS)
                up_of(0, 0, q)

            def products(e, slot, q, split=True):
                if q == 0:
                    weights_ready(e)
                gate_of(e, slot, q)
                up_of(e, slot, q)
                if q == 0:
                    pe.wait_ge(dn_loaded[1 - slot], of(after(e, -1), 8, 16 - 8 * (1 - slot)))
                down(after(e, -1), 1 - slot, q, split)

            products(1, 1, 0)
            gate_of(1, 1, 1)
            transpose_comb(1)
            up_of(1, 1, 1)
            down(0, 0, 1, split=False)
            with pe.Fori(0, E // 2 - 1) as k:
                for slot in (1, 0):
                    e = (k, 2 - slot)
                    for q in range(PE_AHEAD, Q):
                        products(e, slot, q)
                    for q in range(PE_AHEAD):
                        products(after(e, 1), 1 - slot, q)
            for q in range(PE_AHEAD, Q):
                products(E - 1, 1, q, split=False)
            pe.wait_ge(dn_loaded[1], 8 * (E - 2) + 16)
            for q in range(KT):
                down(E - 1, 1, q, split=False)
            for piece in range(2):
                for q in range(KT, Q):
                    down(E - 1, 1, q, False, piece * QUARTER, QUARTER)


def _silu_at_limit():
    import math
    a = ALPHA * LIMIT
    return a / (1.0 + math.exp(-a))


SILU_AT_LIMIT = _silu_at_limit()


def kernel(x, itok_B_0_63, L0_cond_W, L0_cond_b, L0_ffn_router_weight, L0_ffn_router_bias,
           L0_ffn_gate_up_proj, L0_ffn_gate_up_proj_bias, L0_ffn_down_proj, L0_ffn_down_proj_bias):
    import numpy as np
    import concourse.bacc as bacc
    from concourse import mybir as mb
    from concourse.bass_utils import run_bass_kernel_spmd

    x = np.asarray(x)
    bsz, s, d = x.shape
    n = bsz * s
    gu = np.asarray(L0_ffn_gate_up_proj)
    dnw = np.asarray(L0_ffn_down_proj)
    e, i2, _ = gu.shape
    kt = i2 // 2 // P
    gub = np.asarray(L0_ffn_gate_up_proj_bias).reshape(e, 2 * kt, P).transpose(2, 0, 1).reshape(P, e * 2 * kt)
    cond_b = np.zeros((P, d), np.float32)
    cond_b[:L0_cond_b.shape[0]] = np.asarray(L0_cond_b)
    least_gap = np.where(np.tril(np.ones((e, e), bool), -1), 0.0, np.finfo(np.float32).tiny).astype(np.float32)
    arrays = {
        "x_t": x.reshape(n, d).T,
        "cat_ids": np.asarray(itok_B_0_63).reshape(1, bsz),
        "cond_w": np.asarray(L0_cond_W),
        "params": np.concatenate([
            np.asarray(L0_ffn_router_weight).T, gub, np.asarray(L0_ffn_down_proj_bias).T,
            np.broadcast_to(np.asarray(L0_ffn_router_bias).reshape(1, e), (P, e)), cond_b,
            np.eye(P, dtype=np.float32), np.broadcast_to(least_gap.reshape(1, e * e), (P, e * e)),
            np.arange(P, dtype=np.float32).reshape(P, 1)], axis=1),
        "gate_up_w": gu.transpose(0, 2, 1),
        "down_w": dnw.reshape(e, d, kt, P).transpose(0, 3, 2, 1).reshape(e, P, kt * d),
    }
    arrays = {k: np.ascontiguousarray(v) for k, v in arrays.items()}
    nc = bacc.Bacc("TRN2", target_bir_lowering=False, num_devices=1)
    args = [nc.dram_tensor(k, a.shape, mb.dt.from_np(a.dtype), kind="ExternalInput").ap() for k, a in arrays.items()]
    args.append(nc.dram_tensor("out_t", (d, n), mb.dt.float32, kind="ExternalOutput").ap())
    adaln_moe_ffn_kernel(nc, *args)
    got = run_bass_kernel_spmd(nc, [arrays], core_ids=[0]).results[0]["out_t"]
    return np.ascontiguousarray(np.asarray(got).T).reshape(bsz, s, d)
```
